# Optimizing a Trainium2 kernel written in Bass

```python
import numpy as np
import jax
import jax.numpy as jnp

def _softmax(x, axis=-1):
    return jax.nn.softmax(x, axis=axis)

def _gelu(x):
    return jax.nn.gelu(x, approximate=True)

def _silu(x):
    return jax.nn.silu(x)

def _sigmoid(x):
    return jax.nn.sigmoid(x)

def _layernorm(x, axis=-1, eps=1e-05):
    m = jnp.mean(x, axis=axis, keepdims=True)
    v = jnp.var(x, axis=axis, keepdims=True)
    return (x - m) / jnp.sqrt(v + eps)

def _scatter_add(tgt, idx, src, axis=0):
    return tgt.at[idx].add(src)

def _segment_sum(src, seg, n):
    return jax.ops.segment_sum(src, seg, n)
kernel_name = 'mk_gnn_preln_d2_gnn_r64_58d3a8'

def setup_inputs(seed: int=0):
    np.random.seed(seed)
    _w = jnp.asarray

    def _rec_inputs():
        import jax
        import jax.numpy as jnp
        _gk = jax.random.key(seed)
        x = -0.0005121 + 1.001 * jax.random.normal(jax.random.fold_in(_gk, 1), (100000, 32), jnp.float32)
        src = jax.random.randint(jax.random.fold_in(_gk, 2), (50000,), 0, 100000, jnp.int32)
        dst = jnp.minimum((100000 * jax.random.uniform(jax.random.fold_in(_gk, 3), (50000,)) ** 2.0).astype(jnp.int32), 99999)
        _o = jnp.argsort(dst, stable=True)
        src = src[_o]
        dst = dst[_o]
        edge_attr_3 = 0.000549083 + 1.00031 * jax.random.normal(jax.random.fold_in(_gk, 12), (50000, 3), jnp.float32)
        edge_attr_32 = -9.77346e-05 + 0.999888 * jax.random.normal(jax.random.fold_in(_gk, 13), (50000, 32), jnp.float32)
        edge_attr_5 = -0.000325185 + 1.00005 * jax.random.normal(jax.random.fold_in(_gk, 14), (50000, 5), jnp.float32)
        edge_weight1 = 0.000452788 + 0.999756 * jax.random.normal(jax.random.fold_in(_gk, 16), (50000, 1), jnp.float32)
        return (x, src, dst, edge_attr_3, edge_attr_32, edge_attr_5, edge_weight1)
    x, src, dst, edge_attr_3, edge_attr_32, edge_attr_5, edge_weight1 = _rec_inputs()

    def _L0_gnn_setup():
        import jax, jax.numpy as jnp
        import numpy as np
        import math
        M = 8
        COMBOS = [(0, 0, 0), (0, 1, 1), (1, 0, 1), (1, 1, 0), (1, 1, 1), (2, 1, 1)]

        def _cg_coeff(j1, m1, j2, m2, j3, m3):
            if m3 != m1 + m2:
                return 0.0
            f = math.factorial
            vmin = max(0, j2 - j3 - m1, j1 + m2 - j3)
            vmax = min(j1 + j2 - j3, j1 - m1, j2 + m2)
            pref = (2 * j3 + 1) * f(j3 + j1 - j2) * f(j3 - j1 + j2) * f(j1 + j2 - j3) / f(j1 + j2 + j3 + 1)
            pref *= f(j3 + m3) * f(j3 - m3) * f(j1 - m1) * f(j1 + m1) * f(j2 - m2) * f(j2 + m2)
            s = 0.0
            for v in range(vmin, vmax + 1):
                s += (-1) ** v / (f(v) * f(j1 + j2 - j3 - v) * f(j1 - m1 - v) * f(j2 + m2 - v) * f(j3 - j2 + m1 + v) * f(j3 - j1 - m2 + v))
            return math.sqrt(pref) * s

        def _su2_cg(l1, l2, l3):
            C = np.zeros((2 * l1 + 1, 2 * l2 + 1, 2 * l3 + 1), dtype=np.complex128)
            for m1 in range(-l1, l1 + 1):
                for m2 in range(-l2, l2 + 1):
                    m3 = m1 + m2
                    if -l3 <= m3 <= l3:
                        C[m1 + l1, m2 + l2, m3 + l3] = _cg_coeff(l1, m1, l2, m2, l3, m3)
            return C

        def _qmat(l):
            q = np.zeros((2 * l + 1, 2 * l + 1), dtype=np.complex128)
            for m in range(-l, 0):
                q[l + m, l + abs(m)] = 1 / np.sqrt(2)
                q[l + m, l - abs(m)] = -1j / np.sqrt(2)
            q[l, l] = 1.0
            for m in range(1, l + 1):
                q[l + m, l + abs(m)] = (-1) ** m / np.sqrt(2)
                q[l + m, l - abs(m)] = 1j * (-1) ** m / np.sqrt(2)
            return (-1j) ** l * q

        def _so3_cg(l1, l2, l3):
            C = np.einsum('ij,kl,mn,ikn->jlm', _qmat(l1), _qmat(l2), np.conj(_qmat(l3)).T, _su2_cg(l1, l2, l3))
            assert np.abs(C.imag).max() < 1e-06
            C = C.real
            return C / np.linalg.norm(C)
        CG = {c: jnp.asarray(_so3_cg(*c), dtype=jnp.float32) for c in COMBOS}
        N, E = (100000, 25000)
        ks = jax.random.split(jax.random.key(seed), 6)
        return {'node_irreps': jax.random.normal(ks[0], (N, 4 * M), jnp.float32), 'edge_index': jax.random.randint(ks[1], (2, E), 0, N, dtype=jnp.int32), 'sh0': jax.random.normal(ks[2], (E, 1), jnp.float32), 'sh1': jax.random.normal(ks[3], (E, 3), jnp.float32), 'sh2': jax.random.normal(ks[4], (E, 5), jnp.float32), 'W': jax.random.normal(ks[5], (len(COMBOS), M, M), jnp.float32)}
    _L0_gnn_all = _L0_gnn_setup()
    _L0_gnn_in = {k: v for k, v in _L0_gnn_all.items() if k in ('W',)}
    del _L0_gnn_all

    def _L1_gnn_setup():
        import jax, jax.numpy as jnp
        import numpy as np
        N_NODES = 50000
        N_EDGES = 25000
        D_FEAT = 32
        key = jax.random.key(seed)
        k1, k2, k3, k4 = jax.random.split(key, 4)
        node_feat = jax.random.normal(k1, (N_NODES, D_FEAT), dtype=jnp.float32)
        edge_feat = jax.random.normal(k2, (N_EDGES, D_FEAT), dtype=jnp.float32)
        eps = jnp.zeros((1,), dtype=jnp.float32)
        src = jax.random.randint(k3, (N_EDGES,), 0, N_NODES, dtype=jnp.int64)
        dst = jax.random.randint(k4, (N_EDGES,), 0, N_NODES, dtype=jnp.int64)
        return {'node_feat': node_feat, 'edge_feat': edge_feat, 'eps': eps, 'src': src, 'dst': dst}
    _L1_gnn_all = _L1_gnn_setup()
    _L1_gnn_in = {k: v for k, v in _L1_gnn_all.items() if k in ('eps',)}
    del _L1_gnn_all
    return {'x': x, 'src': src, 'dst': dst, 'edge_attr_3': edge_attr_3, 'edge_attr_32': edge_attr_32, 'edge_attr_5': edge_attr_5, 'edge_weight1': edge_weight1, 'L0_gnn_W': _L0_gnn_in['W'], 'L1_gnn_eps': _L1_gnn_in['eps']}

def reference(x, src, dst, edge_attr_3, edge_attr_32, edge_attr_5, edge_weight1, L0_gnn_W, L1_gnn_eps):
    import jax
    import jax.numpy as jnp

    def _L0_gnn_ref(node_irreps, edge_index, sh0, sh1, sh2, W):
        import jax, jax.numpy as jnp
        import numpy as np
        import math
        M = 8
        COMBOS = [(0, 0, 0), (0, 1, 1), (1, 0, 1), (1, 1, 0), (1, 1, 1), (2, 1, 1)]

        def _cg_coeff(j1, m1, j2, m2, j3, m3):
            if m3 != m1 + m2:
                return 0.0
            f = math.factorial
            vmin = max(0, j2 - j3 - m1, j1 + m2 - j3)
            vmax = min(j1 + j2 - j3, j1 - m1, j2 + m2)
            pref = (2 * j3 + 1) * f(j3 + j1 - j2) * f(j3 - j1 + j2) * f(j1 + j2 - j3) / f(j1 + j2 + j3 + 1)
            pref *= f(j3 + m3) * f(j3 - m3) * f(j1 - m1) * f(j1 + m1) * f(j2 - m2) * f(j2 + m2)
            s = 0.0
            for v in range(vmin, vmax + 1):
                s += (-1) ** v / (f(v) * f(j1 + j2 - j3 - v) * f(j1 - m1 - v) * f(j2 + m2 - v) * f(j3 - j2 + m1 + v) * f(j3 - j1 - m2 + v))
            return math.sqrt(pref) * s

        def _su2_cg(l1, l2, l3):
            C = np.zeros((2 * l1 + 1, 2 * l2 + 1, 2 * l3 + 1), dtype=np.complex128)
            for m1 in range(-l1, l1 + 1):
                for m2 in range(-l2, l2 + 1):
                    m3 = m1 + m2
                    if -l3 <= m3 <= l3:
                        C[m1 + l1, m2 + l2, m3 + l3] = _cg_coeff(l1, m1, l2, m2, l3, m3)
            return C

        def _qmat(l):
            q = np.zeros((2 * l + 1, 2 * l + 1), dtype=np.complex128)
            for m in range(-l, 0):
                q[l + m, l + abs(m)] = 1 / np.sqrt(2)
                q[l + m, l - abs(m)] = -1j / np.sqrt(2)
            q[l, l] = 1.0
            for m in range(1, l + 1):
                q[l + m, l + abs(m)] = (-1) ** m / np.sqrt(2)
                q[l + m, l - abs(m)] = 1j * (-1) ** m / np.sqrt(2)
            return (-1j) ** l * q

        def _so3_cg(l1, l2, l3):
            C = np.einsum('ij,kl,mn,ikn->jlm', _qmat(l1), _qmat(l2), np.conj(_qmat(l3)).T, _su2_cg(l1, l2, l3))
            assert np.abs(C.imag).max() < 1e-06
            C = C.real
            return C / np.linalg.norm(C)
        CG = {c: jnp.asarray(_so3_cg(*c), dtype=jnp.float32) for c in COMBOS}
        N, E = (node_irreps.shape[0], edge_index.shape[1])
        src = node_irreps[edge_index[0]]
        feats = {0: src[:, :M][:, :, None], 1: src[:, M:].reshape(E, M, 3)}
        sh = {0: sh0, 1: sh1, 2: sh2}
        msg = {0: jnp.zeros((E, M, 1), node_irreps.dtype), 1: jnp.zeros((E, M, 3), node_irreps.dtype)}
        for idx, (le, ln, lo) in enumerate(COMBOS):
            base = jnp.einsum('ijk,ei,emj->emk', CG[le, ln, lo], sh[le], feats[ln])
            msg[lo] = msg[lo] + jnp.einsum('io,eik->eok', W[idx], base)
        tgt = edge_index[1]
        agg0 = jax.ops.segment_sum(msg[0].reshape(E, M), tgt, num_segments=N)
        agg1 = jax.ops.segment_sum(msg[1].reshape(E, 3 * M), tgt, num_segments=N)
        return jnp.concatenate([agg0, agg1], axis=1)

    def _L1_gnn_ref(node_feat, edge_feat, eps, src, dst):
        import jax, jax.numpy as jnp
        import numpy as np
        N_NODES = 50000
        N_EDGES = 25000
        D_FEAT = 32
        m = jax.nn.relu(node_feat[src] + edge_feat)
        neigh = jax.ops.segment_sum(m, dst, num_segments=node_feat.shape[0])
        return (1.0 + eps[0]) * node_feat + neigh
    edge_index = jnp.stack([src, dst])
    h = jnp.maximum(_layernorm(x, axis=-1), 0.0)
    x = x + _L0_gnn_ref(h, edge_index, edge_weight1, edge_attr_3, edge_attr_5, L0_gnn_W)
    h = jnp.maximum(_layernorm(x, axis=-1), 0.0)
    x = x + _L1_gnn_ref(h, edge_attr_32, L1_gnn_eps, src, dst)
    return x

_drawn_inputs = setup_inputs


def setup_inputs(seed=0):
    import zlib

    import numpy as np

    out = dict(_drawn_inputs(seed))
    spreads = {}
    factors = {}
    for name, (base, spread) in spreads.items():
        noise = np.random.default_rng([zlib.crc32(name.encode()), seed]).standard_normal(out[name].shape)
        drawn = base * np.exp(spread * noise) if base else spread * noise
        out[name] = jnp.asarray(drawn.astype(out[name].dtype))
    for name, factor in factors.items():
        out[name] = (out[name] * factor).astype(out[name].dtype)
    return out
```

```python
import math
from contextlib import ExitStack

import numpy as np
import concourse.bass as bass
import concourse.mybir as mybir

P = 128
NODES, FEAT, EDGES = 100000, 32, 50000
MULT = 8
SPH = 9
EPS_LN = 1e-5

PAIRS_PER_CHUNK = 7
CHUNK = 2 * PAIRS_PER_CHUNK
CHUNKS_PER_BODY = 2
BODY = CHUNK * CHUNKS_PER_BODY
BODY_PAIRS = BODY // 2
BODIES = -(-EDGES // (P * BODY))
TILES = BODIES * BODY
PAIRS = TILES // 2
SPARE = NODES
PAD_DST = NODES + 2 * P
DENSE_ROWS = 56
DENSE_STEPS = 2 * -(-(PAD_DST + 1) // (2 * P * DENSE_ROWS))
ROWS_PER_PART = DENSE_STEPS * DENSE_ROWS
TABLE = P * ROWS_PER_PART
AHEAD = {1: 2, 2: 6}

COMBOS = [(0, 0, 0), (0, 1, 1), (1, 0, 1), (1, 1, 0), (1, 1, 1), (2, 1, 1)]


def clebsch_gordan():
    f = math.factorial

    def coefficient(j1, m1, j2, m2, j3, m3):
        if m3 != m1 + m2:
            return 0.0
        low = max(0, j2 - j3 - m1, j1 + m2 - j3)
        high = min(j1 + j2 - j3, j1 - m1, j2 + m2)
        pref = (2 * j3 + 1) * f(j3 + j1 - j2) * f(j3 - j1 + j2) * f(j1 + j2 - j3) / f(j1 + j2 + j3 + 1)
        pref *= f(j3 + m3) * f(j3 - m3) * f(j1 - m1) * f(j1 + m1) * f(j2 - m2) * f(j2 + m2)
        s = 0.0
        for v in range(low, high + 1):
            s += (-1) ** v / (f(v) * f(j1 + j2 - j3 - v) * f(j1 - m1 - v) * f(j2 + m2 - v)
                              * f(j3 - j2 + m1 + v) * f(j3 - j1 - m2 + v))
        return math.sqrt(pref) * s

    def su2(l1, l2, l3):
        c = np.zeros((2 * l1 + 1, 2 * l2 + 1, 2 * l3 + 1), dtype=np.complex128)
        for m1 in range(-l1, l1 + 1):
            for m2 in range(-l2, l2 + 1):
                if -l3 <= m1 + m2 <= l3:
                    c[m1 + l1, m2 + l2, m1 + m2 + l3] = coefficient(l1, m1, l2, m2, l3, m1 + m2)
        return c

    def real_basis(l):
        q = np.zeros((2 * l + 1, 2 * l + 1), dtype=np.complex128)
        for m in range(-l, 0):
            q[l + m, l + abs(m)] = 1 / np.sqrt(2)
            q[l + m, l - abs(m)] = -1j / np.sqrt(2)
        q[l, l] = 1.0
        for m in range(1, l + 1):
            q[l + m, l + abs(m)] = (-1) ** m / np.sqrt(2)
            q[l + m, l - abs(m)] = 1j * (-1) ** m / np.sqrt(2)
        return (-1j) ** l * q

    out = {}
    for l1, l2, l3 in COMBOS:
        c = np.einsum("ij,kl,mn,ikn->jlm", real_basis(l1), real_basis(l2),
                      np.conj(real_basis(l3)).T, su2(l1, l2, l3)).real
        out[l1, l2, l3] = (c / np.linalg.norm(c)).astype(np.float32)
    return out


def channel(f):
    return (0, f, 0) if f < MULT else (1, (f - MULT) // 3, (f - MULT) % 3)


def cg_table():
    cg = clebsch_gordan()
    sph = [(0, 0)] + [(1, i) for i in range(3)] + [(2, i) for i in range(5)]
    table = np.zeros((FEAT, FEAT, SPH), np.float32)
    for fi in range(FEAT):
        ln, _, j = channel(fi)
        for fo in range(FEAT):
            lo, _, k = channel(fo)
            for s, (le, i) in enumerate(sph):
                if (le, ln, lo) in cg:
                    table[fi, fo, s] = cg[le, ln, lo][i, j, k]
    return table.reshape(FEAT, FEAT * SPH)


W_BLOCKS = [(0, 3), (1, 1), (2, 4), (5, 5)]


def build(nc, x, src, dst, sh, edge_feat, cg, w_rows, eps, x1, out):
    fp32, i32 = mybir.dt.float32, mybir.dt.int32
    ALU, ACT, AX = mybir.AluOpType, mybir.ActivationFunctionType, mybir.AxisListType
    OUTS = FEAT * SPH
    ds = bass.ds

    with ExitStack() as ctx:
        def sb(name, shape, dt=fp32):
            return ctx.enter_context(nc.sbuf_tensor(name, shape, dt))

        def ps(name, shape):
            return ctx.enter_context(nc.psum_tensor(name, shape, fp32))

        def sem(name):
            return ctx.enter_context(nc.semaphore(name))

        sh_all = sb("sh_all", [P, TILES * SPH])
        edge_all = sb("edge_all", [P, TILES * FEAT])
        dst_int = sb("dst_int", [P, TILES], i32)
        dst_all = sb("dst_all", [P, TILES])
        off_spare = sb("off_spare", [P, TILES])
        row_all = sb("row_all", [P, TILES], i32)
        fetched = sb("fetched", [P, TILES * FEAT])
        ident = sb("ident", [P, P])
        earlier = sb("earlier", [P, 3 * P])
        spare_int = sb("spare_int", [P, 2], i32)
        spare = sb("spare", [P, 2])
        cg_sb = sb("cg_sb", [2 * FEAT, OUTS])
        w_sb = sb("w_sb", [2 * FEAT, len(W_BLOCKS) * MULT])
        mix = sb("mix", [2 * FEAT, OUTS])
        ln_eps = sb("ln_eps", [P, 1])
        gin_scale = sb("gin_scale", [P, 1])

        src_ring = sb("src_ring", [P, BODY], i32)
        gather_ring = sb("gather_ring", [P, BODY, FEAT])
        dst_ring = sb("dst_ring", [P, BODY])
        row_ring = sb("row_ring", [P, BODY], i32)
        sum_ring = sb("sum_ring", [P, BODY, FEAT])
        h_ring = sb("h_ring", [P, BODY, FEAT])
        hT = sb("hT", [2 * FEAT, 2, P])
        same = sb("same", [P, 2, 2, 2 * P])
        msg = sb("msg", [P, 2, 2, FEAT])
        prod = sb("prod", [P, 2, FEAT, SPH])
        junk = sb("junk", [P, 3 * P])
        earlier_n = sb("earlier_n", [P, 2])
        shift = sb("shift", [P, 2])
        ln_sum = sb("ln_sum", [P, CHUNK])
        centred = sb("centred", [P, CHUNK, FEAT])
        square = sb("square", [P, CHUNK, FEAT])
        ln_var = sb("ln_var", [P, CHUNK])
        ln_std = sb("ln_std", [P, CHUNK])
        ln_rstd = sb("ln_rstd", [P, CHUNK])
        normed = sb("normed", [P, CHUNK, FEAT])
        D = DENSE_ROWS
        dx = sb("dx", [P, 2, D, FEAT])
        d_out = sb("d_out", [P, 2, D, FEAT])
        d_cen = sb("d_cen", [P, D, FEAT])
        d_sq = sb("d_sq", [P, D, FEAT])
        d_h = sb("d_h", [P, D, FEAT])
        d_sum = sb("d_sum", [P, D])
        d_var = sb("d_var", [P, D])
        d_std = sb("d_std", [P, D])
        d_rstd = sb("d_rstd", [P, D])

        dstT = [ps(f"dstT{i}", [P, 512]) for i in range(2)]
        hT_ps = ps("hT_ps", [P, 512])
        y = [ps(f"y{i}", [P, 2, 512]) for i in range(2)]
        total = ps("total", [P, 512])

        edges_in = sem("edges_in")
        feat_in = sem("feat_in")
        x1_copied = sem("x1_copied")
        masks_ready = sem("masks_ready")
        consts_step = sem("consts_step")
        consts_ready = sem("consts_ready")
        dst_ready = sem("dst_ready")

        names = ["added", "dstT_ready", "hT_ready", "hT_copied", "y_ready", "y_used", "same_ready",
                 "earlier_ready", "shift_ready", "msg_ready", "total_ready", "total_copied",
                 "ring_dst_ready", "summed", "centred_ready", "square_ready", "var_ready", "std_ready",
                 "rstd_ready", "normed_ready", "chunk_ready", "unrelued", "src0", "src1",
                 "gathered0", "gathered1", "fetched0", "fetched1", "rows_ready", "gather_begun", "add_begun"]
        S = {layer: {n: sem(f"l{layer}_{n}") for n in names} for layer in (1, 2)}
        dn = {n: sem("dense_" + n) for n in ["in0", "in1", "summed", "centred", "square", "var", "std",
                                              "rstd", "h", "out", "stored0", "stored1"]}

        block = ctx.enter_context(nc.Block())

        def wait(eng, s, value):
            if isinstance(value, int) and value <= 0:
                return
            eng.wait_ge(s, value)

        def add_landed(i, pair):
            if isinstance(i, int) and i * BODY_PAIRS + pair < 0:
                return 0
            return i * BODY_PAIRS + pair + 2

        def bodies(eng, body, n=BODIES):
            body(0)
            with eng.Fori(1, n) as i:
                body(i)

        def cols(i, k, n, width=1):
            return ds(i * (BODY * width) + k * width, n * width)

        @block.sync
        def _(sp):
            def fetch(layer):
                s = S[layer]
                src_sem = [s["src0"], s["src1"]]
                fetched_sem = [s["fetched0"], s["fetched1"]]
                gathered = [s["gathered0"], s["gathered1"]]
                sp.dma_start(src_ring[:, 0:CHUNK], src[:, 0:CHUNK]).then_inc(src_sem[0], 16)
                with sp.Fori(0, BODIES) as i:
                    for h in range(2):
                        nxt = 1 - h
                        sp.wait_ge(s["gather_begun"], i * 2 + h + 1)
                        sp.dma_start(src_ring[:, nxt * CHUNK:(nxt + 1) * CHUNK],
                                     src[:, cols(i, (h + 1) * CHUNK, CHUNK)]).then_inc(src_sem[nxt], 16)
                        sp.wait_ge(gathered[h], i * (16 * CHUNK) + 16 * CHUNK)
                        sp.dma_start(fetched[:, cols(i, h * CHUNK, CHUNK, FEAT)],
                                     gather_ring[:, h * CHUNK:(h + 1) * CHUNK, :].rearrange("p t f -> p (t f)"))\
                            .then_inc(fetched_sem[h], 16)
                sp.wait_ge(src_sem[0], 16 * (BODIES + 1))

            sp.dma_start(dst_int[:, :], dst).then_inc(edges_in, 16)
            sp.dma_start(cg_sb[0:FEAT, :], cg).then_inc(edges_in, 16)
            sp.dma_start(cg_sb[FEAT:2 * FEAT, :], cg).then_inc(edges_in, 16)
            sp.dma_start(w_sb[:, :], w_rows).then_inc(edges_in, 16)
            sp.dma_start(gin_scale[:, :], eps.to_broadcast([P, 1])).then_inc(edges_in, 16)
            sp.dma_start(sh_all[:, :], sh).then_inc(edges_in, 16)
            sp.dma_start(x1.rearrange("(a b) f -> a (b f)", a=1024),
                         x.rearrange("(a b) f -> a (b f)", a=1024)).then_inc(x1_copied, 16)
            fetch(1)
            sp.dma_start(edge_all[:, :], edge_feat).then_inc(feat_in, 16)
            fetch(2)

        @block.gpsimd
        def _(pool):
            def gather(layer, table, i, h, k):
                s = S[layer]
                t = h * CHUNK + k
                if k == 0:
                    pool.wait_ge(s[f"src{h}"], i * 16 + 16)
                    wait(pool, s[f"fetched{h}"], i * 16)
                    pool.sem_inc(s["gather_begun"], 1)
                pool.indirect_dma_start(gather_ring[:, t, :], None, table,
                                        bass.IndirectOffsetOnAxis(src_ring[:, t:t + 1], 0))\
                    .then_inc(s[f"gathered{h}"], 16)

            def add(layer, table, i, pair):
                s = S[layer]
                pool.wait_ge(s["total_copied"], i * BODY_PAIRS + pair + 1)
                wait(pool, s["added"], i * (32 * BODY_PAIRS) + 32 * pair)
                pool.sem_inc(s["add_begun"], 1)
                for t in (2 * pair, 2 * pair + 1):
                    pool.indirect_dma_start(table, bass.IndirectOffsetOnAxis(row_ring[:, t:t + 1], 0),
                                            sum_ring[:, t, :], None, compute_op=ALU.add)\
                        .then_inc(s["added"], 16)

            def layer_dmas(layer, source, target, wait_for_target):
                ahead = AHEAD[layer]

                def gather_body(i):
                    for t in range(BODY):
                        gather(layer, source, i, t // CHUNK, t % CHUNK)

                def add_body(i):
                    for pair in range(BODY_PAIRS):
                        for t in (2 * pair, 2 * pair + 1):
                            gather(layer, source, i + ahead, t // CHUNK, t % CHUNK)
                        add(layer, target, i, pair)
                bodies(pool, gather_body, ahead)
                wait_for_target()
                bodies(pool, add_body, BODIES - ahead)
                with pool.Fori(BODIES - ahead, BODIES) as i:
                    for pair in range(BODY_PAIRS):
                        add(layer, target, i, pair)
                pool.wait_ge(S[layer]["added"], 32 * PAIRS)

            nc.gpsimd.memset(ident[:, :], 0.0).then_inc(masks_ready, 1)
            nc.gpsimd.memset(earlier[:, :], 1.0).then_inc(masks_ready, 1)
            nc.gpsimd.iota(spare_int[:, :], pattern=[[P, 2]], base=SPARE, channel_multiplier=1)\
                .then_inc(masks_ready, 1)
            pool.wait_ge(masks_ready, 3)
            nc.gpsimd.affine_select(out=ident[:, :], in_=ident[:, :], compare_op=ALU.not_equal, fill=1.0,
                                    base=0, pattern=[[-1, P]], channel_multiplier=1).then_inc(masks_ready, 1)
            for at in (0, 2 * P):
                nc.gpsimd.affine_select(out=earlier[:, at:at + P], in_=earlier[:, at:at + P],
                                        compare_op=ALU.is_gt, fill=0.0, base=0, pattern=[[-1, P]],
                                        channel_multiplier=1).then_inc(masks_ready, 1)

            layer_dmas(1, x, x1, lambda: pool.wait_ge(x1_copied, 16))
            pool.wait_ge(S[1]["fetched0"], 16 * BODIES)
            pool.wait_ge(S[1]["fetched1"], 16 * BODIES)

            def dense_stored():
                pool.wait_ge(dn["stored0"], 16 * (DENSE_STEPS // 2))
                pool.wait_ge(dn["stored1"], 16 * (DENSE_STEPS // 2))
            layer_dmas(2, x1, out, dense_stored)

        @block.scalar
        def _(act):
            def ring_dst(layer, i, h):
                s = S[layer]
                wait(act, s["dstT_ready"], i * BODY_PAIRS + (h - 1) * PAIRS_PER_CHUNK)
                nc.scalar.activation(dst_ring[:, h * CHUNK:(h + 1) * CHUNK],
                                     dst_all[:, cols(i, h * CHUNK, CHUNK)], ACT.Copy)\
                    .then_inc(s["ring_dst_ready"], 1)

            def norm_square(layer, i, h):
                s = S[layer]
                act.wait_ge(s["centred_ready"], i * 2 + h + 1)
                nc.scalar.activation(square[:, :, :], centred[:, :, :], ACT.Square).then_inc(s["square_ready"], 1)

            def norm_std(layer, i, h):
                s = S[layer]
                act.wait_ge(s["var_ready"], i * 2 + h + 1)
                nc.scalar.activation(ln_std[:, :], ln_var[:, :], ACT.Sqrt, bias=ln_eps[:, :],
                                     scale=1.0 / FEAT).then_inc(s["std_ready"], 1)

            def copy_total(layer, i, pair):
                s = S[layer]
                act.wait_ge(s["total_ready"], i * BODY_PAIRS + pair + 1)
                wait(act, s["add_begun"], add_landed(i, pair - BODY_PAIRS))
                nc.scalar.activation(sum_ring[:, 2 * pair:2 * pair + 2, :],
                                     total[:, 0:2 * FEAT].rearrange("p (a f) -> p a f", a=2),
                                     ACT.Copy).then_inc(s["total_copied"], 1)

            def copy_hT(i, pair):
                s = S[1]
                act.wait_ge(s["hT_ready"], i * BODY_PAIRS + pair + 1)
                wait(act, s["y_ready"], i * BODY_PAIRS + pair - 1)
                slot = pair % 2
                nc.scalar.activation(hT[:, slot, :], hT_ps[0:2 * FEAT, 0:P], ACT.Copy)\
                    .then_inc(s["hT_copied"], 1)

            act.wait_ge(consts_ready, 1)
            act.wait_ge(dst_ready, 1)

            def layer1(i):
                ring_dst(1, i, 0)
                norm_square(1, i, 0)
                norm_std(1, i, 0)
                for pair in range(BODY_PAIRS):
                    if pair == 3:
                        ring_dst(1, i, 1)
                        norm_square(1, i, 1)
                        norm_std(1, i, 1)
                    copy_hT(i, pair)
                    if pair:
                        copy_total(1, i, pair - 1)
                copy_total(1, i, BODY_PAIRS - 1)
            bodies(act, layer1)

            act.wait_ge(S[1]["added"], 32 * PAIRS)
            x1_rows = x1.rearrange("(p r) f -> p (r f)", p=P)
            out_rows = out.rearrange("(p r) f -> p (r f)", p=P)

            def dense_load(i, h):
                act.dma_start(dx[:, h, :, :].rearrange("p r f -> p (r f)"),
                              x1_rows[:, ds(i * (2 * D * FEAT) + h * D * FEAT, D * FEAT)])\
                    .then_inc(dn[f"in{h}"], 16)

            dense_load(0, 0)
            dense_load(0, 1)

            def dense(i, last=False):
                for h in range(2):
                    act.wait_ge(dn["centred"], i * 2 + h + 1)
                    nc.scalar.activation(d_sq[:, :, :], d_cen[:, :, :], ACT.Square).then_inc(dn["square"], 1)
                    act.wait_ge(dn["var"], i * 2 + h + 1)
                    nc.scalar.activation(d_std[:, :], d_var[:, :], ACT.Sqrt, bias=ln_eps[:, :],
                                         scale=1.0 / FEAT).then_inc(dn["std"], 1)
                    act.wait_ge(dn["out"], i * 2 + h + 1)
                    act.dma_start(out_rows[:, ds(i * (2 * D * FEAT) + h * D * FEAT, D * FEAT)],
                                  d_out[:, h, :, :].rearrange("p r f -> p (r f)")).then_inc(dn[f"stored{h}"], 16)
                    if not last:
                        dense_load(i + 1, h)
            with act.Fori(0, DENSE_STEPS // 2 - 1) as i:
                dense(i)
            dense(DENSE_STEPS // 2 - 1, last=True)

            act.wait_ge(S[1]["dstT_ready"], PAIRS)

            def relu_message(i, h):
                s = S[2]
                act.wait_ge(s["unrelued"], i * 2 + h + 1)
                wait(act, s["total_ready"], i * BODY_PAIRS + (h - 1) * PAIRS_PER_CHUNK)
                nc.scalar.activation(h_ring[:, h * CHUNK:(h + 1) * CHUNK, :], normed[:, :, :], ACT.Relu)\
                    .then_inc(s["chunk_ready"], 1)

            def layer2(i):
                for h in range(2):
                    ring_dst(2, i, h)
                    norm_square(2, i, h)
                    norm_std(2, i, h)
                    relu_message(i, h)
                    for pair in range(h * PAIRS_PER_CHUNK, (h + 1) * PAIRS_PER_CHUNK):
                        copy_total(2, i, pair)
            bodies(act, layer2)

        @block.vector
        def _(dve):
            bc = lambda ap, shape: ap.to_broadcast(shape)

            nc.vector.memset(ln_eps[:, :], EPS_LN).then_inc(consts_step, 1)
            dve.wait_ge(edges_in, 16 * 6)
            dve.wait_ge(masks_ready, 6)
            cg_v = cg_sb[:, :].rearrange("p (g s) -> p g s", s=SPH)
            mix_v = mix[:, :].rearrange("p (g s) -> p g s", s=SPH)
            w_v = w_sb[:, :].rearrange("p (b o) -> p b o", b=len(W_BLOCKS))
            nc.vector.tensor_tensor(mix_v[:, 0:MULT, :], cg_v[:, 0:MULT, :],
                                    w_v[:, 0, :].unsqueeze(2).to_broadcast([2 * FEAT, MULT, SPH]), ALU.mult)\
                .then_inc(consts_step, 1)
            for blk, s0, s1 in ((1, 0, 1), (2, 1, 4), (3, 4, 9)):
                for k in range(3):
                    nc.vector.tensor_tensor(
                        mix_v[:, MULT + k:FEAT:3, s0:s1], cg_v[:, MULT + k:FEAT:3, s0:s1],
                        w_v[:, blk, :].unsqueeze(2).to_broadcast([2 * FEAT, MULT, s1 - s0]), ALU.mult)\
                        .then_inc(consts_step, 1)
            nc.vector.tensor_copy(dst_all[:, :], dst_int[:, :]).then_inc(consts_step, 1)
            nc.vector.tensor_copy(spare[:, :], spare_int[:, :]).then_inc(consts_step, 1)
            nc.vector.tensor_scalar(gin_scale[:, :], gin_scale[:, :], 1.0, None, ALU.add).then_inc(consts_step, 1)
            dve.wait_ge(consts_step, 14)
            for b in range(2):
                last = nc.vector.tensor_scalar(off_spare[:, b:TILES:2], dst_all[:, b:TILES:2],
                                               spare[:, b:b + 1], None, ALU.subtract)
                last.then_inc(consts_step, 1)
            dve.wait_ge(consts_step, 16)
            dve.sem_inc(consts_ready, 1)
            dve.sem_inc(dst_ready, 1)

            def normalise(layer, i, h):
                s = S[layer]
                c1 = i * 2 + h + 1
                rows = fetched[:, cols(i, h * CHUNK, CHUNK, FEAT)].rearrange("p (t f) -> p t f", f=FEAT)
                wide = [P, CHUNK, FEAT]
                dve.wait_ge(s[f"fetched{h}"], i * 16 + 16)
                nc.vector.tensor_reduce(ln_sum[:, :], rows, axis=AX.X, op=ALU.add).then_inc(s["summed"], 1)
                dve.wait_ge(s["summed"], c1)
                nc.vector.scalar_tensor_tensor(out=centred[:, :, :], in0=ln_sum[:, :].unsqueeze(2).to_broadcast(wide),
                                               scalar=-1.0 / FEAT, in1=rows, op0=ALU.mult, op1=ALU.add)\
                    .then_inc(s["centred_ready"], 1)
                dve.wait_ge(s["square_ready"], c1)
                nc.vector.tensor_reduce(ln_var[:, :], square[:, :, :], axis=AX.X, op=ALU.add)\
                    .then_inc(s["var_ready"], 1)
                dve.wait_ge(s["std_ready"], c1)
                nc.vector.reciprocal(ln_rstd[:, :], ln_std[:, :]).then_inc(s["rstd_ready"], 1)
                dve.wait_ge(s["rstd_ready"], c1)
                if layer == 1:
                    wait(dve, s["hT_ready"], i * BODY_PAIRS + (h - 1) * PAIRS_PER_CHUNK)
                    to, done = h_ring[:, h * CHUNK:(h + 1) * CHUNK, :], s["chunk_ready"]
                else:
                    if not (isinstance(i, int) and i == 0 and h == 0):
                        dve.wait_ge(s["chunk_ready"], c1 - 1)
                    to, done = normed[:, :, :], s["normed_ready"]
                nc.vector.scalar_tensor_tensor(out=to, in0=centred[:, :, :], scalar=0.0,
                                               in1=ln_rstd[:, :].unsqueeze(2).to_broadcast(wide),
                                               op0=ALU.max, op1=ALU.mult).then_inc(done, 1)
                if layer == 2:
                    feats = edge_all[:, cols(i, h * CHUNK, CHUNK, FEAT)].rearrange("p (t f) -> p t f", f=FEAT)
                    dve.wait_ge(s["normed_ready"], c1)
                    nc.vector.tensor_tensor(normed[:, :, :], normed[:, :, :], feats, ALU.add)\
                        .then_inc(s["unrelued"], 1)

            def compare(layer, i, pair):
                s = S[layer]
                slot = pair % 2
                dve.wait_ge(s["dstT_ready"], i * BODY_PAIRS + pair + 1)
                wait(dve, s["total_ready"], i * BODY_PAIRS + pair - 1)
                for b in range(2):
                    last = nc.vector.tensor_scalar(same[:, slot, b, :], dstT[slot][:, 0:2 * P],
                                                   dst_all[:, cols(i, 2 * pair + b, 1)], None, ALU.is_equal)
                last.then_inc(s["same_ready"], 1)

            def count_earlier(i, pair):
                s = S[1]
                slot = pair % 2
                for b in range(2):
                    n = (b + 1) * P
                    last = nc.vector.scalar_tensor_tensor(
                        out=junk[:, b * P:b * P + n], in0=dstT[slot][:, 0:n], scalar=dst_all[:, cols(i, 2 * pair + b, 1)],
                        in1=earlier[:, b * P:b * P + n], op0=ALU.is_equal, op1=ALU.mult,
                        accum_out=earlier_n[:, b:b + 1])
                    last.then_inc(s["earlier_ready"], 1)

            def layer1(i):
                normalise(1, i, 0)
                s = S[1]
                for pair in range(BODY_PAIRS):
                    if pair == 3:
                        normalise(1, i, 1)
                    slot = pair % 2
                    q1 = i * BODY_PAIRS + pair + 1
                    t2 = cols(i, 2 * pair, 2)
                    dve.wait_ge(s["dstT_ready"], q1)
                    count_earlier(i, pair)
                    compare(1, i, pair)
                    dve.wait_ge(s["earlier_ready"], i * (2 * BODY_PAIRS) + 2 * pair + 2)
                    nc.vector.scalar_tensor_tensor(out=shift[:, :], in0=earlier_n[:, :], scalar=0.0,
                                                   in1=off_spare[:, t2], op0=ALU.is_gt, op1=ALU.mult)\
                        .then_inc(s["shift_ready"], 1)
                    dve.wait_ge(s["y_ready"], q1)
                    sph = sh_all[:, cols(i, 2 * pair, 2, SPH)].rearrange("p (t o s) -> p t o s", t=2, o=1)
                    nc.vector.tensor_tensor(prod[:, :, :, :],
                                            y[slot][:, :, 0:OUTS].rearrange("p t (g s) -> p t g s", s=SPH),
                                            sph.to_broadcast([P, 2, FEAT, SPH]), ALU.mult)\
                        .then_inc(s["y_used"], 1)
                    dve.wait_ge(s["shift_ready"], q1)
                    nc.vector.tensor_tensor(row_all[:, t2], dst_all[:, t2], shift[:, :], ALU.subtract)
                    wait(dve, s["add_begun"], add_landed(i, pair - BODY_PAIRS))
                    nc.vector.tensor_tensor(row_ring[:, 2 * pair:2 * pair + 2], dst_all[:, t2], shift[:, :],
                                            ALU.subtract).then_inc(s["rows_ready"], 1)
                    dve.wait_ge(s["y_used"], q1)
                    nc.vector.tensor_reduce(msg[:, slot, :, :], prod[:, :, :, :], axis=AX.X, op=ALU.add)\
                        .then_inc(s["msg_ready"], 1)
            bodies(dve, layer1)

            wide = [P, D, FEAT]

            def dense(i):
                for h in range(2):
                    k1 = i * 2 + h + 1
                    dve.wait_ge(dn[f"in{h}"], i * 16 + 16)
                    nc.vector.tensor_reduce(d_sum[:, :], dx[:, h, :, :], axis=AX.X, op=ALU.add)\
                        .then_inc(dn["summed"], 1)
                    dve.wait_ge(dn["summed"], k1)
                    nc.vector.scalar_tensor_tensor(out=d_cen[:, :, :], in0=d_sum[:, :].unsqueeze(2).to_broadcast(wide),
                                                   scalar=-1.0 / FEAT, in1=dx[:, h, :, :],
                                                   op0=ALU.mult, op1=ALU.add).then_inc(dn["centred"], 1)
                    dve.wait_ge(dn["square"], k1)
                    nc.vector.tensor_reduce(d_var[:, :], d_sq[:, :, :], axis=AX.X, op=ALU.add)\
                        .then_inc(dn["var"], 1)
                    dve.wait_ge(dn["std"], k1)
                    nc.vector.reciprocal(d_rstd[:, :], d_std[:, :]).then_inc(dn["rstd"], 1)
                    dve.wait_ge(dn["rstd"], k1)
                    nc.vector.scalar_tensor_tensor(out=d_h[:, :, :], in0=d_cen[:, :, :], scalar=0.0,
                                                   in1=d_rstd[:, :].unsqueeze(2).to_broadcast(wide),
                                                   op0=ALU.max, op1=ALU.mult).then_inc(dn["h"], 1)
                    dve.wait_ge(dn["h"], k1)
                    wait(dve, dn[f"stored{h}"], i * 16)
                    nc.vector.scalar_tensor_tensor(out=d_out[:, h, :, :], in0=d_h[:, :, :],
                                                   scalar=gin_scale[:, :], in1=dx[:, h, :, :],
                                                   op0=ALU.mult, op1=ALU.add).then_inc(dn["out"], 1)
            bodies(dve, dense, DENSE_STEPS // 2)

            dve.wait_ge(feat_in, 16)
            dve.wait_ge(S[1]["total_ready"], PAIRS)
            dve.wait_ge(S[1]["added"], 32 * PAIRS)

            def ring_rows(i, h):
                wait(dve, S[2]["add_begun"], add_landed(i, (h - 1) * PAIRS_PER_CHUNK - 1))
                nc.vector.tensor_copy(row_ring[:, h * CHUNK:(h + 1) * CHUNK], row_all[:, cols(i, h * CHUNK, CHUNK)])\
                    .then_inc(S[2]["rows_ready"], 1)

            def layer2(i):
                for h in range(2):
                    normalise(2, i, h)
                    ring_rows(i, h)
                    for pair in range(h * PAIRS_PER_CHUNK, (h + 1) * PAIRS_PER_CHUNK):
                        compare(2, i, pair)
            bodies(dve, layer2)

        @block.tensor
        def _(pe):
            def spread_dst(layer, i, pair):
                s = S[layer]
                slot = pair % 2
                if pair % PAIRS_PER_CHUNK == 0:
                    pe.wait_ge(s["ring_dst_ready"], i * 2 + pair // PAIRS_PER_CHUNK + 1)
                wait(pe, s["same_ready"], i * BODY_PAIRS + pair - 1)
                for b in range(2):
                    t = 2 * pair + b
                    last = nc.tensor.matmul(dstT[slot][:, b * P:(b + 1) * P],
                                            dst_ring[:, t:t + 1].to_broadcast([P, P]), ident[:, :],
                                            start=True, stop=True)
                last.then_inc(s["dstT_ready"], 1)

            def expand(i, pair):
                s = S[1]
                slot = pair % 2
                nc.tensor.transpose(hT_ps[0:2 * FEAT, 0:P],
                                    h_ring[:, 2 * pair:2 * pair + 2, :].rearrange("p t f -> p (t f)"),
                                    ident[:, :]).then_inc(s["hT_ready"], 1)
                pe.wait_ge(s["hT_copied"], i * BODY_PAIRS + pair + 1)
                wait(pe, s["y_used"], i * BODY_PAIRS + pair - 1)
                for b in range(2):
                    rows = slice(b * FEAT, (b + 1) * FEAT)
                    last = nc.tensor.matmul(y[slot][:, b, 0:OUTS], hT[rows, slot, :], mix[rows, :],
                                            start=True, stop=True)
                last.then_inc(s["y_ready"], 1)

            def combine(layer, i, pair):
                s = S[layer]
                slot = pair % 2
                pe.wait_ge(s["same_ready"], i * BODY_PAIRS + pair + 1)
                if layer == 1:
                    pe.wait_ge(s["msg_ready"], i * BODY_PAIRS + pair + 1)
                wait(pe, s["total_copied"], i * BODY_PAIRS + pair)
                for a in range(2):
                    to = total[:, a * FEAT:(a + 1) * FEAT]
                    for b in range(2):
                        m = msg[:, slot, b, :] if layer == 1 else h_ring[:, 2 * pair + b, :]
                        last = nc.tensor.matmul(to, same[:, slot, b, a * P:(a + 1) * P], m,
                                                start=(b == 0), stop=(b == 1))
                last.then_inc(s["total_ready"], 1)

            pe.wait_ge(consts_ready, 1)

            def layer1(i):
                for pair in range(BODY_PAIRS):
                    if pair % PAIRS_PER_CHUNK == 0:
                        pe.wait_ge(S[1]["chunk_ready"], i * 2 + pair // PAIRS_PER_CHUNK + 1)
                    wait(pe, S[1]["hT_copied"], i * BODY_PAIRS + pair)
                    spread_dst(1, i, pair)
                    expand(i, pair)
                    if pair:
                        combine(1, i, pair - 1)
                combine(1, i, BODY_PAIRS - 1)
            bodies(pe, layer1)

            pe.wait_ge(S[1]["total_copied"], PAIRS)
            pe.wait_ge(S[1]["same_ready"], PAIRS)

            def layer2(i):
                for h in range(2):
                    for pair in range(h * PAIRS_PER_CHUNK, (h + 1) * PAIRS_PER_CHUNK):
                        spread_dst(2, i, pair)
                        if pair % PAIRS_PER_CHUNK == 0:
                            pe.wait_ge(S[2]["chunk_ready"], i * 2 + h + 1)
                        else:
                            combine(2, i, pair - 1)
                    combine(2, i, (h + 1) * PAIRS_PER_CHUNK - 1)
            bodies(pe, layer2)


def kernel(x, src, dst, edge_attr_3, edge_attr_32, edge_attr_5, edge_weight1, L0_gnn_W, L1_gnn_eps):
    import concourse.bacc as bacc
    from concourse.bass_utils import run_bass_kernel_spmd

    def padded(a, rows, fill=0):
        a = np.asarray(a)
        out = np.full((rows,) + a.shape[1:], fill, a.dtype)
        out[:len(a)] = a
        return out

    slots = P * TILES
    src_cols = np.zeros((P, TILES + CHUNK), np.int32)
    src_cols[:, :TILES] = padded(src, slots).reshape(P, TILES)
    sh = np.concatenate([np.asarray(edge_weight1), np.asarray(edge_attr_3), np.asarray(edge_attr_5)], axis=1)
    w = np.asarray(L0_gnn_W)
    w_rows = np.stack([np.stack([w[W_BLOCKS[b][channel(f)[0]], channel(f)[1]] for b in range(len(W_BLOCKS))])
                       for f in range(FEAT)]).reshape(FEAT, -1)
    arrays = {
        "x": padded(x, TABLE),
        "src": src_cols,
        "dst": padded(dst, slots, PAD_DST).reshape(P, TILES),
        "sh": padded(sh, slots).reshape(P, TILES * SPH),
        "edge_feat": padded(edge_attr_32, slots).reshape(P, TILES * FEAT),
        "cg": cg_table(),
        "w_rows": np.concatenate([w_rows, w_rows]),
        "eps": np.asarray(L1_gnn_eps).reshape(1, 1),
    }
    nc = bacc.Bacc("TRN2", target_bir_lowering=False, num_devices=1)
    feeds, args = {}, []
    for name, a in arrays.items():
        feeds[f"in_{name}"] = np.ascontiguousarray(a)
        args.append(nc.dram_tensor(f"in_{name}", a.shape, mybir.dt.from_np(a.dtype), kind="ExternalInput").ap())
    x1 = nc.dram_tensor("x1", (TABLE, FEAT), mybir.dt.float32, kind="Internal").ap()
    out = nc.dram_tensor("out", (TABLE, FEAT), mybir.dt.float32, kind="ExternalOutput").ap()
    build(nc, *args, x1, out)
    result = run_bass_kernel_spmd(nc, [feeds], core_ids=[0])
    return result.results[0]["out"][:NODES]
```

```python
import math
from contextlib import ExitStack

import numpy as np
import concourse.bass as bass
import concourse.mybir as mybir

P = 128
NODES, FEAT, EDGES = 100000, 32, 50000
MULT = 8
SPH = 9
EPS_LN = 1e-5

CHUNK = 14
BODY = 2 * CHUNK
BODIES = -(-EDGES // (P * BODY))
TILES = BODIES * BODY
GROUP = {1: 2, 2: 4}
BODY_GROUPS = {l: BODY // k for l, k in GROUP.items()}
GROUPS = {l: TILES // k for l, k in GROUP.items()}

LOT = 7
LOTS = TILES // LOT
RING_LOTS = 4
BODY_LOTS = {1: 4, 2: 2}
FULL_BODIES = BODIES - 2
LAST_LOTS = {1: 0, 2: 3}
AHEAD_LOTS = {l: LOTS - FULL_BODIES * BODY_LOTS[l] - LAST_LOTS[l] for l in GROUP}
RING_TILES = RING_LOTS * LOT

SPARE = NODES
PAD_DST = NODES + max(GROUP.values()) * P
DENSE_ROWS = 33
DENSE_RING = 4
DENSE_STEPS = DENSE_RING * -(-(PAD_DST + 1) // (P * DENSE_ROWS * DENSE_RING))
ROWS_PER_PART = DENSE_STEPS * DENSE_ROWS
TABLE = P * ROWS_PER_PART
COPY_PIECES = 8
EDGE_PIECES = DENSE_STEPS // DENSE_RING - 2

COMBOS = [(0, 0, 0), (0, 1, 1), (1, 0, 1), (1, 1, 0), (1, 1, 1), (2, 1, 1)]


def clebsch_gordan():
    f = math.factorial

    def coefficient(j1, m1, j2, m2, j3, m3):
        if m3 != m1 + m2:
            return 0.0
        low = max(0, j2 - j3 - m1, j1 + m2 - j3)
        high = min(j1 + j2 - j3, j1 - m1, j2 + m2)
        pref = (2 * j3 + 1) * f(j3 + j1 - j2) * f(j3 - j1 + j2) * f(j1 + j2 - j3) / f(j1 + j2 + j3 + 1)
        pref *= f(j3 + m3) * f(j3 - m3) * f(j1 - m1) * f(j1 + m1) * f(j2 - m2) * f(j2 + m2)
        s = 0.0
        for v in range(low, high + 1):
            s += (-1) ** v / (f(v) * f(j1 + j2 - j3 - v) * f(j1 - m1 - v) * f(j2 + m2 - v)
                              * f(j3 - j2 + m1 + v) * f(j3 - j1 - m2 + v))
        return math.sqrt(pref) * s

    def su2(l1, l2, l3):
        c = np.zeros((2 * l1 + 1, 2 * l2 + 1, 2 * l3 + 1), dtype=np.complex128)
        for m1 in range(-l1, l1 + 1):
            for m2 in range(-l2, l2 + 1):
                if -l3 <= m1 + m2 <= l3:
                    c[m1 + l1, m2 + l2, m1 + m2 + l3] = coefficient(l1, m1, l2, m2, l3, m1 + m2)
        return c

    def real_basis(l):
        q = np.zeros((2 * l + 1, 2 * l + 1), dtype=np.complex128)
        for m in range(-l, 0):
            q[l + m, l + abs(m)] = 1 / np.sqrt(2)
            q[l + m, l - abs(m)] = -1j / np.sqrt(2)
        q[l, l] = 1.0
        for m in range(1, l + 1):
            q[l + m, l + abs(m)] = (-1) ** m / np.sqrt(2)
            q[l + m, l - abs(m)] = 1j * (-1) ** m / np.sqrt(2)
        return (-1j) ** l * q

    out = {}
    for l1, l2, l3 in COMBOS:
        c = np.einsum("ij,kl,mn,ikn->jlm", real_basis(l1), real_basis(l2),
                      np.conj(real_basis(l3)).T, su2(l1, l2, l3)).real
        out[l1, l2, l3] = (c / np.linalg.norm(c)).astype(np.float32)
    return out


def channel(f):
    return (0, f, 0) if f < MULT else (1, (f - MULT) // 3, (f - MULT) % 3)


def cg_table():
    cg = clebsch_gordan()
    sph = [(0, 0)] + [(1, i) for i in range(3)] + [(2, i) for i in range(5)]
    table = np.zeros((FEAT, FEAT, SPH), np.float32)
    for fi in range(FEAT):
        ln, _, j = channel(fi)
        for fo in range(FEAT):
            lo, _, k = channel(fo)
            for s, (le, i) in enumerate(sph):
                if (le, ln, lo) in cg:
                    table[fi, fo, s] = cg[le, ln, lo][i, j, k]
    return table.reshape(FEAT, FEAT * SPH)


W_BLOCKS = [(0, 3), (1, 1), (2, 4), (5, 5)]


def build(nc, x, src, dst, sh, edge_feat, cg, w_rows, eps, x1, out):
    fp32, bf16, i32 = mybir.dt.float32, mybir.dt.bfloat16, mybir.dt.int32
    ALU, ACT, AX = mybir.AluOpType, mybir.ActivationFunctionType, mybir.AxisListType
    OUTS = FEAT * SPH
    G_MAX = max(GROUP.values())
    ds = bass.ds

    with ExitStack() as ctx:
        def sb(name, shape, dt=fp32):
            return ctx.enter_context(nc.sbuf_tensor(name, shape, dt))

        def ps(name, shape, dt=fp32):
            return ctx.enter_context(nc.psum_tensor(name, shape, dt))

        def sem(name):
            return ctx.enter_context(nc.semaphore(name))

        edge_all = sb("edge_all", [P, TILES * FEAT])
        sh_all = edge_all[:, 0:TILES * SPH]
        dst_int = sb("dst_int", [P, TILES], i32)
        dst_all = sb("dst_all", [P, TILES])
        dst_parts = sb("dst_parts", [P, 2, TILES], bf16)
        off_spare = sb("off_spare", [P, TILES])
        fetched = sb("fetched", [P, TILES * FEAT])
        ident = sb("ident", [P, P], bf16)
        earlier = sb("earlier", [P, G_MAX * P], bf16)
        spare_int = sb("spare_int", [P, G_MAX], i32)
        spare = sb("spare", [P, G_MAX])
        cg_sb = sb("cg_sb", [P, OUTS])
        w_sb = sb("w_sb", [P, len(W_BLOCKS) * MULT])
        mix = sb("mix", [P, OUTS])
        mix_rest = sb("mix_rest", [P, OUTS])
        mix_part = [sb(f"mix_part{i}", [P, OUTS], bf16) for i in range(3)]
        mix_high = sb("mix_high", [P, OUTS], bf16)
        mix_low = sb("mix_low", [P, OUTS], bf16)
        ln_eps = sb("ln_eps", [P, 1])
        gin_scale = sb("gin_scale", [P, 1])

        src_ring = sb("src_ring", [P, RING_TILES], i32)
        gather_ring = sb("gather_ring", [P, RING_TILES, FEAT])
        dst_ring = sb("dst_ring", [P, 2, BODY], bf16)
        row_ring = sb("row_ring", [P, BODY], i32)
        sum_ring = sb("sum_ring", [P, BODY, FEAT])
        h_high = sb("h_high", [P, BODY, 4, FEAT], bf16)
        h_low = sb("h_low", [P, BODY, 2, FEAT], bf16)
        hT = sb("hT", [P, 2, 3 * P], bf16)
        same = {1: sb("same1", [P, 2, GROUP[1], GROUP[1] * P]),
                2: sb("same2", [P, 2, GROUP[2], GROUP[2] * P], bf16)}
        msg = sb("msg", [P, 2, GROUP[1], FEAT])
        msg_parts = sb("msg_parts", [P, BODY, 3, FEAT], bf16)
        prod = sb("prod", [P, GROUP[1], FEAT, SPH])
        junk = sb("junk", [P, G_MAX * (G_MAX + 1) // 2 * P], bf16)
        earlier_n = sb("earlier_n", [P, G_MAX])
        shift = sb("shift", [P, G_MAX])
        ln_sum = sb("ln_sum", [P, CHUNK])
        centred = sb("centred", [P, CHUNK, FEAT])
        square = sb("square", [P, CHUNK, FEAT])
        ln_var = sb("ln_var", [P, CHUNK])
        ln_std = sb("ln_std", [P, CHUNK])
        ln_rstd = sb("ln_rstd", [P, CHUNK])
        normed = sb("normed", [P, CHUNK, FEAT])
        rest = sb("rest", [P, CHUNK, FEAT])
        D = DENSE_ROWS
        dx = sb("dx", [P, DENSE_RING, D, FEAT])
        d_out = sb("d_out", [P, DENSE_RING, D, FEAT])
        d_cen = sb("d_cen", [P, 2, D, FEAT])
        d_sq = sb("d_sq", [P, D, FEAT])
        d_sum = sb("d_sum", [P, 2, D])
        d_var = sb("d_var", [P, D])
        d_std = sb("d_std", [P, D])
        d_rstd = sb("d_rstd", [P, D])

        dstT = [ps(f"dstT{i}", [P, 512]) for i in range(2)]
        hT_ps = ps("hT_ps", [P, 1024], bf16)
        y = [ps(f"y{i}", [P, 2, 512]) for i in range(2)]
        total = ps("total", [P, 512])
        dst_banks = {1: [dstT[g % 2] for g in range(BODY_GROUPS[1])],
                     2: [dstT[g % 2] for g in range(BODY_GROUPS[2] - 1)] + [y[0][:, 0, :]]}

        edges_in = sem("edges_in")
        feat_in = sem("feat_in")
        x1_copied = sem("x1_copied")
        masks_ready = sem("masks_ready")
        consts_step = sem("consts_step")
        consts_ready = sem("consts_ready")

        names = ["src_in", "gather_begun", "gathered0", "gathered1", "fetched",
                 "ring_dst_ready", "dstT_ready", "same_ready", "earlier_ready", "shift_ready", "rows_ready",
                 "summed", "centred_ready", "square_ready", "var_ready", "std_ready", "rstd_ready",
                 "h_ready", "normed_ready", "part1_ready", "rest_ready", "part2_ready", "chunk_ready",
                 "hT_ready", "hT_copied", "y_ready", "y_used", "msg_ready",
                 "total_ready", "total_copied", "add_begun", "added"]
        S = {layer: {n: sem(f"l{layer}_{n}") for n in names} for layer in (1, 2)}
        dn = {n: sem("dense_" + n) for n in ["summed", "centred", "square", "var", "std", "rstd", "h", "out"]}
        dense_in = [sem(f"dense_in{r}") for r in range(DENSE_RING)]
        dense_stored = [sem(f"dense_stored{r}") for r in range(DENSE_RING)]

        block = ctx.enter_context(nc.Block())

        def wait(eng, s, value):
            if isinstance(value, int) and value <= 0:
                return
            eng.wait_ge(s, value)

        def group_no(layer, i, g):
            return i * BODY_GROUPS[layer] + g

        def slot_free(layer, i, g):
            behind = 1 if g == 0 and BODY_GROUPS[layer] % 2 else 2
            return i * BODY_GROUPS[layer] + (g - behind + 1)

        def bank_free(layer, i, g):
            groups = BODY_GROUPS[layer]
            behind = next(k for k in range(1, groups + 1)
                          if dst_banks[layer][(g - k) % groups] is dst_banks[layer][g])
            return i * groups + (g - behind + 1)

        def half_free(layer, i, h):
            groups = -(-CHUNK * (h % 2 + 1) // GROUP[layer])
            return i * BODY_GROUPS[layer] + ((h // 2 - 1) * BODY_GROUPS[layer] + groups)

        def first_of_chunk(layer, g):
            last = (g + 1) * GROUP[layer] - 1
            return last // CHUNK if g == 0 or (last - GROUP[layer]) // CHUNK != last // CHUNK else None

        def add_landed(layer, i, g):
            if isinstance(i, int) and group_no(layer, i, g) < 0:
                return 0
            return i * BODY_GROUPS[layer] + (g + 2)

        def bodies(eng, body, n=BODIES):
            body(0)
            with eng.Fori(1, n) as i:
                body(i)

        def chunked(eng, body, n=BODIES):
            body(0, False)
            with eng.Fori(1, n - 1) as i:
                body(i, False)
            body(n - 1, True)

        def cols(i, k, n, width=1):
            return ds(i * (BODY * width) + k * width, n * width)

        @block.sync
        def _(sp):
            def load_constants():
                sp.dma_start(dst_int[:, :], dst).then_inc(edges_in, 16)
                sp.dma_start(cg_sb[:, :], cg).then_inc(edges_in, 16)
                sp.dma_start(w_sb[:, :], w_rows).then_inc(edges_in, 16)
                sp.dma_start(gin_scale[:, :], eps.to_broadcast([P, 1])).then_inc(edges_in, 16)
                sp.dma_start(sh_all, sh).then_inc(edges_in, 16)

            def copy_x(piece):
                n = TABLE // COPY_PIECES
                rows = slice(piece * n, (piece + 1) * n)
                sp.dma_start(x1[rows, :].rearrange("(a b) f -> a (b f)", a=P),
                             x[rows, :].rearrange("(a b) f -> a (b f)", a=P)).then_inc(x1_copied, 16)

            def fetch(layer):
                s = S[layer]
                sp.dma_start(src_ring[:, :], src[:, 0:RING_TILES]).then_inc(s["src_in"], 16)
                if layer == 1:
                    load_constants()
                    copy_x(0)

                def move_lot(n, n_half, place):
                    tiles = slice(place * LOT, (place + 1) * LOT)
                    sp.wait_ge(s[f"gathered{place % 2}"], n_half * (16 * LOT) + 16 * LOT)
                    wait(sp, s["fetched"], n * 16)
                    sp.dma_start(fetched[:, ds(n * (LOT * FEAT), LOT * FEAT)],
                                 gather_ring[:, tiles, :].rearrange("p t f -> p (t f)")).then_inc(s["fetched"], 16)
                    sp.wait_ge(s["src_in"], n * 16 + 16)
                    sp.dma_start(src_ring[:, tiles], src[:, ds(n * LOT + RING_TILES, LOT)])\
                        .then_inc(s["src_in"], 16)

                straight = 2 * RING_LOTS
                for n in range(straight):
                    if layer == 1 and n + 1 < COPY_PIECES:
                        copy_x(n + 1)
                    move_lot(n, n // 2, n % RING_LOTS)
                with sp.Fori(2, LOTS // RING_LOTS) as j:
                    for m in range(RING_LOTS):
                        move_lot(j * RING_LOTS + m, j * (RING_LOTS // 2) + m // 2, m)
                sp.wait_ge(s["src_in"], 16 * (LOTS + 1))

            fetch(1)
            fetch(2)

        @block.gpsimd
        def _(pool):
            def gather(layer, table, n, n_half, place, k):
                s = S[layer]
                t = place * LOT + k
                if k == 0:
                    if isinstance(n, int) and n < RING_LOTS:
                        pool.wait_ge(s["src_in"], 16)
                    else:
                        pool.wait_ge(s["src_in"], n * 16 + (32 - 16 * RING_LOTS))
                        pool.wait_ge(s["fetched"], n * 16 + (16 - 16 * RING_LOTS))
                    wait(pool, s[f"gathered{place % 2}"], n_half * (16 * LOT))
                    pool.sem_inc(s["gather_begun"], 1)
                pool.indirect_dma_start(gather_ring[:, t, :], None, table,
                                        bass.IndirectOffsetOnAxis(src_ring[:, t:t + 1], 0))\
                    .then_inc(s[f"gathered{place % 2}"], 16)

            def add(layer, table, i, g):
                s, size = S[layer], GROUP[layer]
                pool.wait_ge(s["total_copied"], group_no(layer, i, g) + 1)
                wait(pool, s["added"], i * (16 * BODY) + 16 * size * g)
                pool.sem_inc(s["add_begun"], 1)
                for t in range(size * g, size * (g + 1)):
                    pool.indirect_dma_start(table, bass.IndirectOffsetOnAxis(row_ring[:, t:t + 1], 0),
                                            sum_ring[:, t, :], None, compute_op=ALU.add)\
                        .then_inc(s["added"], 16)

            def layer_dmas(layer, source, target, wait_for_target):
                per_body, ahead, groups = BODY_LOTS[layer], AHEAD_LOTS[layer], BODY_GROUPS[layer]

                def gather_lot(n, n_half, place):
                    for k in range(LOT):
                        gather(layer, source, n, n_half, place, k)
                for n in range(RING_LOTS):
                    gather_lot(n, n // 2, n)
                rings = ahead // RING_LOTS
                if rings > 1:
                    with pool.Fori(1, rings) as j:
                        for m in range(RING_LOTS):
                            gather_lot(j * RING_LOTS + m, j * (RING_LOTS // 2) + m // 2, m)
                for n in range(rings * RING_LOTS, ahead):
                    gather_lot(n, n // 2, n % RING_LOTS)
                wait_for_target()

                def gathers(i, k, done, upto):
                    for t in range(done, upto):
                        n = ahead + t // LOT
                        gather(layer, source, i * per_body + n, i * (per_body // 2) + n // 2,
                               (k * per_body + n) % RING_LOTS, t % LOT)

                def add_bodies(j):
                    bodies_in_ring = RING_LOTS // per_body
                    for k in range(bodies_in_ring):
                        i = j * bodies_in_ring + k
                        for g in range(groups):
                            gathers(i, k, per_body * LOT * g // groups, per_body * LOT * (g + 1) // groups)
                            add(layer, target, i, g)
                bodies(pool, add_bodies, FULL_BODIES * per_body // RING_LOTS)
                most, size = LAST_LOTS[layer] * LOT, GROUP[layer]
                for g in range(groups):
                    gathers(FULL_BODIES, 0, min(size * g, most), min(size * (g + 1), most))
                    add(layer, target, FULL_BODIES, g)
                for g in range(groups):
                    add(layer, target, FULL_BODIES + 1, g)
                pool.wait_ge(S[layer]["added"], 16 * TILES)

            nc.gpsimd.memset(ident[:, :], 0.0).then_inc(masks_ready, 1)
            nc.gpsimd.memset(earlier[:, :], 1.0).then_inc(masks_ready, 1)
            nc.gpsimd.iota(spare_int[:, :], pattern=[[P, G_MAX]], base=SPARE, channel_multiplier=1)\
                .then_inc(masks_ready, 1)
            pool.wait_ge(masks_ready, 3)
            nc.gpsimd.affine_select(out=ident[:, :], in_=ident[:, :], compare_op=ALU.not_equal, fill=1.0,
                                    base=0, pattern=[[-1, P]], channel_multiplier=1).then_inc(masks_ready, 1)
            own = earlier[:, (G_MAX - 1) * P:G_MAX * P]
            nc.gpsimd.affine_select(out=own, in_=own, compare_op=ALU.is_gt, fill=0.0, base=0,
                                    pattern=[[-1, P]], channel_multiplier=1).then_inc(masks_ready, 1)

            layer_dmas(1, x, x1, lambda: pool.wait_ge(x1_copied, 16 * COPY_PIECES))
            pool.wait_ge(S[1]["fetched"], 16 * LOTS)

            def dense_done():
                for stored in dense_stored:
                    pool.wait_ge(stored, 16 * (DENSE_STEPS // DENSE_RING))
            layer_dmas(2, x1, out, dense_done)

        @block.scalar
        def _(act):
            def ring_dst(layer, i, h):
                s = S[layer]
                at = (h % 2) * CHUNK
                wait(act, s["dstT_ready"], half_free(layer, i, h))
                nc.scalar.activation(dst_ring[:, :, at:at + CHUNK],
                                     dst_parts[:, :, cols(i, h * CHUNK, CHUNK)], ACT.Copy)\
                    .then_inc(s["ring_dst_ready"], 1)

            def norm_square(layer, i, h):
                s = S[layer]
                act.wait_ge(s["centred_ready"], i * 2 + (h + 1))
                nc.scalar.activation(square[:, :, :], centred[:, :, :], ACT.Square).then_inc(s["square_ready"], 1)

            def norm_std(layer, i, h):
                s = S[layer]
                act.wait_ge(s["var_ready"], i * 2 + (h + 1))
                nc.scalar.activation(ln_std[:, :], ln_var[:, :], ACT.Sqrt, bias=ln_eps[:, :],
                                     scale=1.0 / FEAT).then_inc(s["std_ready"], 1)

            def part1(layer, i, h):
                s = S[layer]
                at = slice((h % 2) * CHUNK, (h % 2 + 1) * CHUNK)
                act.wait_ge(s["normed_ready"], i * 2 + (h + 1))
                if layer == 1:
                    wait(act, s["hT_ready"], half_free(1, i, h))
                    nc.scalar.activation(h_low[:, at, 0, :], normed[:, :, :], ACT.Copy)
                    nc.scalar.activation(h_high[:, at, 0:2, :],
                                         normed[:, :, :].unsqueeze(2).to_broadcast([P, CHUNK, 2, FEAT]), ACT.Copy)\
                        .then_inc(s["part1_ready"], 1)
                else:
                    wait(act, s["total_ready"], half_free(2, i, h))
                    nc.scalar.activation(msg_parts[:, at, 0, :], normed[:, :, :], ACT.Relu)\
                        .then_inc(s["part1_ready"], 1)

            def part2(layer, i, h):
                s = S[layer]
                at = slice((h % 2) * CHUNK, (h % 2 + 1) * CHUNK)
                act.wait_ge(s["rest_ready"], i * 2 + (h + 1))
                if layer == 1:
                    nc.scalar.activation(h_high[:, at, 2:4, :],
                                         rest[:, :, :].unsqueeze(2).to_broadcast([P, CHUNK, 2, FEAT]), ACT.Copy)\
                        .then_inc(s["part2_ready"], 1)
                else:
                    nc.scalar.activation(msg_parts[:, at, 1, :], rest[:, :, :], ACT.Copy)\
                        .then_inc(s["part2_ready"], 1)

            steps_at = {
                1: {7 * h + k: (h + 1, step) for h in range(2)
                    for k, step in ((2, [norm_square]), (3, [norm_std]), (4, [part1]), (5, [part2]), (6, [ring_dst]))},
                2: {4 * h + k: (h + 1, step) for h in range(2)
                    for k, step in ((0, [norm_square, norm_std]), (1, [part1, part2]), (2, [ring_dst]))},
            }

            def prepare(layer, i, g, last):
                if g in steps_at[layer]:
                    h, steps = steps_at[layer][g]
                    if not (last and h == 2):
                        for step in steps:
                            step(layer, i, h)

            def first_chunk(layer):
                for step in (ring_dst, norm_square, norm_std, part1, part2):
                    step(layer, 0, 0)

            def copy_total(layer, i, g):
                s, size = S[layer], GROUP[layer]
                act.wait_ge(s["total_ready"], group_no(layer, i, g) + 1)
                wait(act, s["add_begun"], add_landed(layer, i, g - BODY_GROUPS[layer]))
                nc.scalar.activation(sum_ring[:, size * g:size * (g + 1), :],
                                     total[:, 0:size * FEAT].rearrange("p (a f) -> p a f", f=FEAT),
                                     ACT.Copy).then_inc(s["total_copied"], 1)

            def copy_hT(i, g):
                s = S[1]
                act.wait_ge(s["hT_ready"], group_no(1, i, g) + 1)
                wait(act, s["y_ready"], slot_free(1, i, g))
                nc.scalar.activation(hT[:, g % 2, :], hT_ps[:, 0:3 * P], ACT.Copy).then_inc(s["hT_copied"], 1)

            act.wait_ge(consts_ready, 1)

            def layer1(i, last):
                for g in range(BODY_GROUPS[1]):
                    prepare(1, i, g, last)
                    copy_hT(i, g)
                    if g:
                        copy_total(1, i, g - 1)
                copy_total(1, i, BODY_GROUPS[1] - 1)
            first_chunk(1)
            chunked(act, layer1)

            act.wait_ge(S[1]["added"], 16 * TILES)
            x1_rows = x1.rearrange("(p r) f -> p (r f)", p=P)
            out_rows = out.rearrange("(p r) f -> p (r f)", p=P)

            def dense_cols(i, r):
                return ds(i * (DENSE_RING * D * FEAT) + r * D * FEAT, D * FEAT)

            def dense_load(i, r):
                act.dma_start(dx[:, r, :, :].rearrange("p r f -> p (r f)"), x1_rows[:, dense_cols(i, r)])\
                    .then_inc(dense_in[r], 16)

            def load_edges(i):
                n = TILES * FEAT // EDGE_PIECES
                act.dma_start(edge_all[:, ds(i * n - n, n)], edge_feat[:, ds(i * n - n, n)]).then_inc(feat_in, 16)

            def dense(i, last):
                if not isinstance(i, int):
                    load_edges(i)
                for r in range(DENSE_RING):
                    k1 = i * DENSE_RING + (r + 1)
                    act.wait_ge(dn["centred"], k1)
                    nc.scalar.activation(d_sq[:, :, :], d_cen[:, r % 2, :, :], ACT.Square).then_inc(dn["square"], 1)
                    act.wait_ge(dn["var"], k1)
                    nc.scalar.activation(d_std[:, :], d_var[:, :], ACT.Sqrt, bias=ln_eps[:, :],
                                         scale=1.0 / FEAT).then_inc(dn["std"], 1)
                    act.wait_ge(dn["out"], k1)
                    act.dma_start(out_rows[:, dense_cols(i, r)],
                                  d_out[:, r, :, :].rearrange("p r f -> p (r f)")).then_inc(dense_stored[r], 16)
                    if not last:
                        dense_load(i + 1, r)
            for r in range(DENSE_RING):
                dense_load(0, r)
            act.wait_ge(S[1]["y_used"], GROUPS[1])
            chunked(act, dense, DENSE_STEPS // DENSE_RING)

            act.wait_ge(S[1]["dstT_ready"], GROUPS[1])

            def layer2(i, last):
                for g in range(BODY_GROUPS[2]):
                    prepare(2, i, g, last)
                    copy_total(2, i, g)
            first_chunk(2)
            chunked(act, layer2)

        @block.vector
        def _(dve):
            nc.vector.memset(ln_eps[:, :], EPS_LN).then_inc(consts_step, 1)
            dve.wait_ge(edges_in, 16 * 5)
            dve.wait_ge(masks_ready, 5)
            cg_v = cg_sb[:, :].rearrange("p (g s) -> p g s", s=SPH)
            mix_v = mix[:, :].rearrange("p (g s) -> p g s", s=SPH)
            w_v = w_sb[:, :].rearrange("p (b o) -> p b o", b=len(W_BLOCKS))
            nc.vector.tensor_tensor(mix_v[:, 0:MULT, :], cg_v[:, 0:MULT, :],
                                    w_v[:, 0, :].unsqueeze(2).to_broadcast([P, MULT, SPH]), ALU.mult)\
                .then_inc(consts_step, 1)
            for blk, s0, s1 in ((1, 0, 1), (2, 1, 4), (3, 4, 9)):
                for k in range(3):
                    nc.vector.tensor_tensor(
                        mix_v[:, MULT + k:FEAT:3, s0:s1], cg_v[:, MULT + k:FEAT:3, s0:s1],
                        w_v[:, blk, :].unsqueeze(2).to_broadcast([P, MULT, s1 - s0]), ALU.mult)\
                        .then_inc(consts_step, 1)
            nc.vector.tensor_copy(dst_all[:, :], dst_int[:, :]).then_inc(consts_step, 1)
            nc.vector.tensor_copy(spare[:, :], spare_int[:, :]).then_inc(consts_step, 1)
            nc.vector.tensor_scalar(gin_scale[:, :], gin_scale[:, :], 1.0, None, ALU.add).then_inc(consts_step, 1)
            dve.wait_ge(consts_step, 14)
            for b in range(G_MAX):
                nc.vector.tensor_scalar(off_spare[:, b:TILES:G_MAX], dst_all[:, b:TILES:G_MAX],
                                        spare[:, b:b + 1], None, ALU.subtract).then_inc(consts_step, 1)
            nc.vector.tensor_copy(dst_parts[:, 0, :], dst_all[:, :]).then_inc(consts_step, 1)
            nc.vector.tensor_copy(mix_part[0][:, :], mix[:, :]).then_inc(consts_step, 1)
            at = 16 + G_MAX
            dve.wait_ge(consts_step, at)
            nc.vector.tensor_tensor(dst_parts[:, 1, :], dst_all[:, :], dst_parts[:, 0, :], ALU.subtract)\
                .then_inc(consts_step, 1)
            nc.vector.tensor_tensor(mix_rest[:, :], mix[:, :], mix_part[0][:, :], ALU.subtract)\
                .then_inc(consts_step, 1)
            dve.wait_ge(consts_step, at + 2)
            nc.vector.tensor_copy(mix_part[1][:, :], mix_rest[:, :]).then_inc(consts_step, 1)
            dve.wait_ge(consts_step, at + 3)
            nc.vector.tensor_tensor(mix_part[2][:, :], mix_rest[:, :], mix_part[1][:, :], ALU.subtract)\
                .then_inc(consts_step, 1)
            dve.wait_ge(consts_step, at + 4)
            for to, parts in ((mix_high, (0, 1, 0, 1)), (mix_low, (2, 0, 2, 0))):
                for n, part in enumerate(parts):
                    rows = slice(n * FEAT, (n + 1) * FEAT)
                    nc.vector.tensor_copy(to[rows, :], mix_part[part][rows, :]).then_inc(consts_step, 1)
            dve.wait_ge(consts_step, at + 12)
            dve.sem_inc(consts_ready, 1)

            wide = [P, CHUNK, FEAT]

            def centre(layer, i, h):
                s = S[layer]
                rows = fetched[:, cols(i, h * CHUNK, CHUNK, FEAT)].rearrange("p (t f) -> p t f", f=FEAT)
                dve.wait_ge(s["fetched"], i * (16 * (BODY // LOT)) + 16 * -(-(h + 1) * CHUNK // LOT))
                nc.vector.tensor_reduce(ln_sum[:, :], rows, axis=AX.X, op=ALU.add).then_inc(s["summed"], 1)
                dve.wait_ge(s["summed"], i * 2 + (h + 1))
                nc.vector.scalar_tensor_tensor(out=centred[:, :, :], in0=ln_sum[:, :].unsqueeze(2).to_broadcast(wide),
                                               scalar=-1.0 / FEAT, in1=rows, op0=ALU.mult, op1=ALU.add)\
                    .then_inc(s["centred_ready"], 1)

            def variance(layer, i, h):
                s = S[layer]
                dve.wait_ge(s["square_ready"], i * 2 + (h + 1))
                nc.vector.tensor_reduce(ln_var[:, :], square[:, :, :], axis=AX.X, op=ALU.add)\
                    .then_inc(s["var_ready"], 1)

            def scale(layer, i, h):
                s = S[layer]
                n1 = i * 2 + (h + 1)
                dve.wait_ge(s["std_ready"], n1)
                nc.vector.reciprocal(ln_rstd[:, :], ln_std[:, :]).then_inc(s["rstd_ready"], 1)
                dve.wait_ge(s["rstd_ready"], n1)
                nc.vector.scalar_tensor_tensor(out=normed[:, :, :], in0=centred[:, :, :], scalar=0.0,
                                               in1=ln_rstd[:, :].unsqueeze(2).to_broadcast(wide),
                                               op0=ALU.max, op1=ALU.mult)\
                    .then_inc(s["normed_ready" if layer == 1 else "h_ready"], 1)
                if layer == 2:
                    feats = edge_all[:, cols(i, h * CHUNK, CHUNK, FEAT)].rearrange("p (t f) -> p t f", f=FEAT)
                    dve.wait_ge(s["h_ready"], n1)
                    nc.vector.tensor_tensor(normed[:, :, :], normed[:, :, :], feats, ALU.add)\
                        .then_inc(s["normed_ready"], 1)

            def leave1(layer, i, h):
                s = S[layer]
                at = slice((h % 2) * CHUNK, (h % 2 + 1) * CHUNK)
                part = h_high[:, at, 0, :] if layer == 1 else msg_parts[:, at, 0, :]
                dve.wait_ge(s["part1_ready"], i * 2 + (h + 1))
                nc.vector.scalar_tensor_tensor(out=rest[:, :, :], in0=normed[:, :, :], scalar=0.0, in1=part,
                                               op0=ALU.max, op1=ALU.subtract).then_inc(s["rest_ready"], 1)

            def part3(layer, i, h):
                s = S[layer]
                at = slice((h % 2) * CHUNK, (h % 2 + 1) * CHUNK)
                second = h_high[:, at, 2, :] if layer == 1 else msg_parts[:, at, 1, :]
                third = h_low[:, at, 1, :] if layer == 1 else msg_parts[:, at, 2, :]
                dve.wait_ge(s["part2_ready"], i * 2 + (h + 1))
                nc.vector.tensor_tensor(third, rest[:, :, :], second, ALU.subtract).then_inc(s["chunk_ready"], 1)

            steps_at = {
                1: {(7 * h + k, 0): (h + 1, step) for h in range(2)
                    for k, step in ((1, centre), (2, variance), (3, scale), (5, leave1), (6, part3))},
                2: {(4 * h + k, half): (h + 1, step) for h in range(2)
                    for k, half, step in ((0, 0, centre), (0, 1, variance), (1, 0, scale), (1, 1, leave1),
                                          (2, 0, part3))},
            }

            def prepare(layer, i, g, half, last):
                if (g, half) in steps_at[layer]:
                    h, step = steps_at[layer][g, half]
                    if not (last and h == 2):
                        step(layer, i, h)

            def first_chunk(layer):
                for step in (centre, variance, scale, leave1, part3):
                    step(layer, 0, 0)

            def compare(layer, i, g):
                s, size, slot = S[layer], GROUP[layer], g % 2
                wait(dve, s["total_ready"], slot_free(layer, i, g))
                for b in range(size):
                    last = nc.vector.tensor_scalar(same[layer][:, slot, b, :], dst_banks[layer][g][:, 0:size * P],
                                                   dst_all[:, cols(i, size * g + b, 1)], None, ALU.is_equal)
                last.then_inc(s["same_ready"], 1)

            def count_earlier(layer, i, g):
                s, size = S[layer], GROUP[layer]
                dve.wait_ge(s["dstT_ready"], group_no(layer, i, g) + 1)
                for b in range(size):
                    n, at = (b + 1) * P, b * (b + 1) // 2 * P
                    nc.vector.scalar_tensor_tensor(
                        out=junk[:, at:at + n], in0=dst_banks[layer][g][:, 0:n], scalar=dst_all[:, cols(i, size * g + b, 1)],
                        in1=earlier[:, (G_MAX - 1 - b) * P:G_MAX * P], op0=ALU.is_equal, op1=ALU.mult,
                        accum_out=earlier_n[:, b:b + 1]).then_inc(s["earlier_ready"], 1)

            def shift_rows(layer, i, g):
                s, size = S[layer], GROUP[layer]
                dve.wait_ge(s["earlier_ready"], i * BODY + size * (g + 1))
                nc.vector.scalar_tensor_tensor(out=shift[:, 0:size], in0=earlier_n[:, 0:size], scalar=0.0,
                                               in1=off_spare[:, cols(i, size * g, size)],
                                               op0=ALU.is_gt, op1=ALU.mult).then_inc(s["shift_ready"], 1)

            def choose_rows(layer, i, g):
                s, size = S[layer], GROUP[layer]
                dve.wait_ge(s["shift_ready"], group_no(layer, i, g) + 1)
                wait(dve, s["add_begun"], add_landed(layer, i, g - BODY_GROUPS[layer]))
                nc.vector.tensor_tensor(row_ring[:, size * g:size * (g + 1)], dst_all[:, cols(i, size * g, size)],
                                        shift[:, 0:size], ALU.subtract).then_inc(s["rows_ready"], 1)

            def layer1(i, last):
                s = S[1]
                for g in range(BODY_GROUPS[1]):
                    prepare(1, i, g, 0, last)
                    slot = g % 2
                    q1 = group_no(1, i, g) + 1
                    count_earlier(1, i, g)
                    compare(1, i, g)
                    shift_rows(1, i, g)
                    dve.wait_ge(s["y_ready"], q1)
                    sph = sh_all[:, cols(i, 2 * g, 2, SPH)].rearrange("p (t o s) -> p t o s", t=2, o=1)
                    nc.vector.tensor_tensor(prod[:, :, :, :],
                                            y[slot][:, :, 0:OUTS].rearrange("p t (g s) -> p t g s", s=SPH),
                                            sph.to_broadcast([P, 2, FEAT, SPH]), ALU.mult)\
                        .then_inc(s["y_used"], 1)
                    choose_rows(1, i, g)
                    dve.wait_ge(s["y_used"], q1)
                    nc.vector.tensor_reduce(msg[:, slot, :, :], prod[:, :, :, :], axis=AX.X, op=ALU.add)\
                        .then_inc(s["msg_ready"], 1)
            first_chunk(1)
            chunked(dve, layer1)

            dense_wide = [P, D, FEAT]

            def dense_centre(i, r):
                nxt, r = divmod(r, DENSE_RING)
                dve.wait_ge(dense_in[r], i * 16 + 16 * (nxt + 1))
                nc.vector.tensor_reduce(d_sum[:, r % 2, :], dx[:, r, :, :], axis=AX.X, op=ALU.add)\
                    .then_inc(dn["summed"], 1)
                dve.wait_ge(dn["summed"], i * DENSE_RING + (nxt * DENSE_RING + r + 1))
                nc.vector.scalar_tensor_tensor(out=d_cen[:, r % 2, :, :],
                                               in0=d_sum[:, r % 2, :].unsqueeze(2).to_broadcast(dense_wide),
                                               scalar=-1.0 / FEAT, in1=dx[:, r, :, :],
                                               op0=ALU.mult, op1=ALU.add).then_inc(dn["centred"], 1)

            def dense(i, last):
                for r in range(DENSE_RING):
                    k1 = i * DENSE_RING + (r + 1)
                    if not (last and r == DENSE_RING - 1):
                        dense_centre(i, r + 1)
                    dve.wait_ge(dn["square"], k1)
                    nc.vector.tensor_reduce(d_var[:, :], d_sq[:, :, :], axis=AX.X, op=ALU.add)\
                        .then_inc(dn["var"], 1)
                    dve.wait_ge(dn["std"], k1)
                    nc.vector.reciprocal(d_rstd[:, :], d_std[:, :]).then_inc(dn["rstd"], 1)
                    dve.wait_ge(dn["rstd"], k1)
                    nc.vector.scalar_tensor_tensor(out=d_cen[:, r % 2, :, :], in0=d_cen[:, r % 2, :, :], scalar=0.0,
                                                   in1=d_rstd[:, :].unsqueeze(2).to_broadcast(dense_wide),
                                                   op0=ALU.max, op1=ALU.mult).then_inc(dn["h"], 1)
                    dve.wait_ge(dn["h"], k1)
                    wait(dve, dense_stored[r], i * 16)
                    nc.vector.scalar_tensor_tensor(out=d_out[:, r, :, :], in0=d_cen[:, r % 2, :, :],
                                                   scalar=gin_scale[:, :], in1=dx[:, r, :, :],
                                                   op0=ALU.mult, op1=ALU.add).then_inc(dn["out"], 1)
            dense_centre(0, 0)
            chunked(dve, dense, DENSE_STEPS // DENSE_RING)

            dve.wait_ge(feat_in, 16 * EDGE_PIECES)
            dve.wait_ge(S[1]["added"], 16 * TILES)

            def layer2(i, last):
                for g in range(BODY_GROUPS[2]):
                    prepare(2, i, g, 0, last)
                    count_earlier(2, i, g)
                    shift_rows(2, i, g)
                    prepare(2, i, g, 1, last)
                    choose_rows(2, i, g)
                    compare(2, i, g)
            first_chunk(2)
            chunked(dve, layer2)

        @block.tensor
        def _(pe):
            def spread_dst(layer, i, g):
                s, size = S[layer], GROUP[layer]
                if (h := first_of_chunk(layer, g)) is not None:
                    pe.wait_ge(s["ring_dst_ready"], i * 2 + (h + 1))
                wait(pe, s["same_ready"], bank_free(layer, i, g))
                for t in range(size * g, size * (g + 1)):
                    at = (t - size * g) * P
                    for part in range(2):
                        last = nc.tensor.matmul(dst_banks[layer][g][:, at:at + P],
                                                dst_ring[:, part, t:t + 1].to_broadcast([P, P]), ident[:, :],
                                                start=(part == 0), stop=(part == 1))
                last.then_inc(s["dstT_ready"], 1)

            def expand(i, g):
                s, slot = S[1], g % 2
                for b in range(2):
                    nc.tensor.transpose(hT_ps[:, b * P:(b + 1) * P],
                                        h_high[:, 2 * g + b, :, :].rearrange("p a f -> p (a f)"), ident[:, :])
                nc.tensor.transpose(hT_ps[:, 2 * P:3 * P],
                                    h_low[:, 2 * g:2 * g + 2, :, :].rearrange("p t a f -> p (t a f)"),
                                    ident[:, :]).then_inc(s["hT_ready"], 1)
                pe.wait_ge(s["hT_copied"], group_no(1, i, g) + 1)
                wait(pe, s["y_used"], slot_free(1, i, g))
                for b in range(2):
                    nc.tensor.matmul(y[slot][:, b, 0:OUTS], hT[:, slot, b * P:(b + 1) * P], mix_high[:, :],
                                     start=True, stop=False)
                    rows = slice(b * 2 * FEAT, (b + 1) * 2 * FEAT)
                    last = nc.tensor.matmul(y[slot][:, b, 0:OUTS], hT[rows, slot, 2 * P:3 * P], mix_low[rows, :],
                                            start=False, stop=True)
                last.then_inc(s["y_ready"], 1)

            def combine(layer, i, g):
                s, size, slot = S[layer], GROUP[layer], g % 2
                pe.wait_ge(s["same_ready"], group_no(layer, i, g) + 1)
                if layer == 1:
                    pe.wait_ge(s["msg_ready"], group_no(layer, i, g) + 1)
                wait(pe, s["total_copied"], group_no(layer, i, g))
                for a in range(size):
                    to = total[:, a * FEAT:(a + 1) * FEAT]
                    cols_a = slice(a * P, (a + 1) * P)
                    if layer == 1:
                        terms = [(same[1][:, slot, b, cols_a], msg[:, slot, b, :]) for b in range(size)]
                    else:
                        terms = [(same[2][:, slot, b, cols_a], msg_parts[:, size * g + b, part, :])
                                 for b in range(size) for part in range(3)]
                    for n, (lhsT, rhs) in enumerate(terms):
                        last = nc.tensor.matmul(to, lhsT, rhs, start=(n == 0), stop=(n == len(terms) - 1))
                last.then_inc(s["total_ready"], 1)

            pe.wait_ge(consts_ready, 1)

            def layer1(i):
                for g in range(BODY_GROUPS[1]):
                    if (h := first_of_chunk(1, g)) is not None:
                        pe.wait_ge(S[1]["chunk_ready"], i * 2 + (h + 1))
                    wait(pe, S[1]["hT_copied"], group_no(1, i, g))
                    spread_dst(1, i, g)
                    expand(i, g)
                    if g:
                        combine(1, i, g - 1)
                combine(1, i, BODY_GROUPS[1] - 1)
            bodies(pe, layer1)

            pe.wait_ge(S[1]["total_copied"], GROUPS[1])
            pe.wait_ge(S[1]["same_ready"], GROUPS[1])
            pe.wait_ge(S[1]["y_used"], GROUPS[1])

            def layer2(i, last):
                for g in range(BODY_GROUPS[2]):
                    if g + 1 < BODY_GROUPS[2]:
                        spread_dst(2, i, g + 1)
                    elif not last:
                        spread_dst(2, i + 1, 0)
                    if (h := first_of_chunk(2, g)) is not None:
                        pe.wait_ge(S[2]["chunk_ready"], i * 2 + (h + 1))
                    combine(2, i, g)
            spread_dst(2, 0, 0)
            chunked(pe, layer2)


def kernel(x, src, dst, edge_attr_3, edge_attr_32, edge_attr_5, edge_weight1, L0_gnn_W, L1_gnn_eps):
    import concourse.bacc as bacc
    from concourse.bass_utils import run_bass_kernel_spmd

    def padded(a, rows, fill=0):
        a = np.asarray(a)
        out = np.full((rows,) + a.shape[1:], fill, a.dtype)
        out[:len(a)] = a
        return out

    slots = P * TILES
    src_cols = np.zeros((P, TILES + RING_TILES), np.int32)
    src_cols[:, :TILES] = padded(src, slots).reshape(P, TILES)
    sh = np.concatenate([np.asarray(edge_weight1), np.asarray(edge_attr_3), np.asarray(edge_attr_5)], axis=1)
    w = np.asarray(L0_gnn_W)
    w_rows = np.stack([np.stack([w[W_BLOCKS[b][channel(f)[0]], channel(f)[1]] for b in range(len(W_BLOCKS))])
                       for f in range(FEAT)]).reshape(FEAT, -1)
    arrays = {
        "x": padded(x, TABLE),
        "src": src_cols,
        "dst": padded(dst, slots, PAD_DST).reshape(P, TILES),
        "sh": padded(sh, slots).reshape(P, TILES * SPH),
        "edge_feat": padded(edge_attr_32, slots).reshape(P, TILES * FEAT),
        "cg": np.tile(cg_table(), (P // FEAT, 1)),
        "w_rows": np.tile(w_rows, (P // FEAT, 1)),
        "eps": np.asarray(L1_gnn_eps).reshape(1, 1),
    }
    nc = bacc.Bacc("TRN2", target_bir_lowering=False, num_devices=1)
    feeds, args = {}, []
    for name, a in arrays.items():
        feeds[f"in_{name}"] = np.ascontiguousarray(a)
        args.append(nc.dram_tensor(f"in_{name}", a.shape, mybir.dt.from_np(a.dtype), kind="ExternalInput").ap())
    x1 = nc.dram_tensor("x1", (TABLE, FEAT), mybir.dt.float32, kind="Internal").ap()
    out = nc.dram_tensor("out", (TABLE, FEAT), mybir.dt.float32, kind="ExternalOutput").ap()
    build(nc, *args, x1, out)
    result = run_bass_kernel_spmd(nc, [feeds], core_ids=[0])
    return result.results[0]["out"][:NODES]
```
